# Optimizing a Trainium2 kernel written in Bass

```python
import numpy as np
import jax
import jax.numpy as jnp

def _softmax(x, axis=-1):
    return jax.nn.softmax(x, axis=axis)

def _gelu(x):
    return jax.nn.gelu(x, approximate=True)

def _silu(x):
    return jax.nn.silu(x)

def _sigmoid(x):
    return jax.nn.sigmoid(x)

def _layernorm(x, axis=-1, eps=1e-05):
    m = jnp.mean(x, axis=axis, keepdims=True)
    v = jnp.var(x, axis=axis, keepdims=True)
    return (x - m) / jnp.sqrt(v + eps)

def _scatter_add(tgt, idx, src, axis=0):
    return tgt.at[idx].add(src)

def _segment_sum(src, seg, n):
    return jax.ops.segment_sum(src, seg, n)
kernel_name = 'mk_rec_standalone_d1_rec_r8_078547'

def setup_inputs(seed: int=0):
    np.random.seed(seed)
    _w = jnp.asarray

    def _rec_inputs():
        import jax
        import jax.numpy as jnp
        _rk = jax.random.key(seed)
        r_inputs = -4.11716e-05 + 1 * jax.random.normal(jax.random.fold_in(_rk, 1), (2048, 64, 256), jnp.float32)
        return r_inputs
    r_inputs = _rec_inputs()

    def _L0_rec_setup():
        import jax, jax.numpy as jnp
        import numpy as np
        B, N, D = (1024, 64, 256)
        key = jax.random.key(seed)
        inputs = jax.random.normal(key, (B, N, D), dtype=jnp.float32)
        return {'inputs': inputs}
    _L0_rec_all = _L0_rec_setup()
    _L0_rec_in = {k: v for k, v in _L0_rec_all.items() if k in ()}
    del _L0_rec_all
    return {'r_inputs': r_inputs}

def reference(r_inputs):
    import jax
    import jax.numpy as jnp

    def _L0_rec_ref(inputs):
        import jax, jax.numpy as jnp
        import numpy as np
        B, N, D = (1024, 64, 256)
        Z = jnp.einsum('bnd,bmd->bnm', inputs, inputs)
        n = inputs.shape[1]
        li, lj = jnp.tril_indices(n, k=-1)
        return Z[:, li, lj]
    y = _L0_rec_ref(r_inputs)
    return y

_drawn_inputs = setup_inputs


def setup_inputs(seed=0):
    import zlib

    import numpy as np

    out = dict(_drawn_inputs(seed))
    spreads = {}
    factors = {}
    for name, (base, spread) in spreads.items():
        noise = np.random.default_rng([zlib.crc32(name.encode()), seed]).standard_normal(out[name].shape)
        drawn = base * np.exp(spread * noise) if base else spread * noise
        out[name] = jnp.asarray(drawn.astype(out[name].dtype))
    for name, factor in factors.items():
        out[name] = (out[name] * factor).astype(out[name].dtype)
    return out
```

```python
from contextlib import ExitStack

import concourse.bass as bass
from concourse import mybir

F32 = mybir.dt.float32
NOT_EQUAL = mybir.AluOpType.not_equal

PARTS = 128
HALF = PARTS // 2
BLOCK = 32


def first_column(i):
    return i * (i - 1) // 2


def is_zero(value):
    return isinstance(value, int) and value == 0


def gram_lower_triangle(nc: bass.Bass, x: bass.AP, y: bass.AP):
    BATCHES, ROWS, DIM = x.shape
    PACKED = y.shape[1]
    SIDES = 2
    RUN = DIM // 2
    KEPT = RUN // 2
    KSTEPS = KEPT // BLOCK
    PAIRS = 8
    SLOTS = PAIRS * (ROWS // BLOCK)
    GROUP_PAIRS = PARTS
    RING = 4
    TILES = GROUP_PAIRS // PAIRS
    QUARTETS = TILES // RING
    GROUPS = BATCHES // (SIDES * GROUP_PAIRS)
    PER_CHUNK = 4
    CHUNKS = ROWS // PER_CHUNK
    CHUNK_BANKS = 4
    KEEP_LAG = 2
    UNPAIR_TILES = 2
    CHUNKS_PER_TILE = CHUNKS // UNPAIR_TILES

    with ExitStack() as stack:
        def sbuf(name, shape):
            return stack.enter_context(nc.sbuf_tensor(name, shape, F32))

        def psum(name, shape):
            return stack.enter_context(nc.psum_tensor(name, shape, F32))

        def semaphore(name):
            return stack.enter_context(nc.semaphore(name))

        x_in = sbuf("x_in", [PARTS, RING, SIDES, SLOTS, RUN])
        x_turned = sbuf("x_turned", [PARTS, RING, SIDES * PAIRS, KSTEPS, ROWS])
        products = sbuf("products", [PARTS, ROWS, GROUP_PAIRS])
        packed_rows = sbuf("packed_rows", [PARTS, SIDES, PACKED])
        identity = sbuf("identity", [PARTS, PARTS])
        product_banks = [psum(f"product_bank{k}", [PARTS, PAIRS, ROWS]) for k in range(RING)]
        unpaired_banks = [psum(f"unpaired_bank{k}", [PARTS, PER_CHUNK, SIDES, ROWS]) for k in range(CHUNK_BANKS)]

        low_loaded = [semaphore(f"low_loaded{k}") for k in range(RING)]
        high_loaded = [semaphore(f"high_loaded{k}") for k in range(RING)]
        crossed = semaphore("crossed")
        turned = semaphore("turned")
        multiplied = semaphore("multiplied")
        kept = semaphore("kept")
        unpaired = semaphore("unpaired")
        packed = semaphore("packed")
        stored = semaphore("stored")
        zeroed = semaphore("zeroed")
        identity_ready = semaphore("identity_ready")

        block = stack.enter_context(nc.Block())

        def walk(engine, quartet):
            quartet(0, 0, None)
            with engine.Fori(1, QUARTETS) as q:
                quartet(0, q, None)
            quartet(1, 0, 0)
            with engine.Fori(1, GROUPS - 1) as group:
                with engine.Fori(1, QUARTETS) as q:
                    quartet(group, q, None)
                quartet(group + 1, 0, group)
            with engine.Fori(1, QUARTETS) as q:
                quartet(GROUPS - 1, q, None)

        def load_tile(engine, side, first, k, loaded):
            for d_half in range(2):
                at = side * HALF + d_half * BLOCK
                source = x[bass.ds(first, PAIRS), :, d_half * RUN:(d_half + 1) * RUN].rearrange(
                    "b (h r) d -> r (b h) d", r=BLOCK)
                engine.dma_start(x_in[at:at + BLOCK, k, side], source).then_inc(loaded[k], 16)

        def loads(engine, side, loaded):
            def quartet(group, q, last_group):
                n = group * QUARTETS + q
                for k in range(RING):
                    if not is_zero(n):
                        engine.wait_ge(turned, n * RING + k - RING + 1)
                    first = (group * SIDES + side) * GROUP_PAIRS + (q * RING + k) * PAIRS
                    load_tile(engine, side, first, k, loaded)
            walk(engine, quartet)

        @block.sync
        def _(sync):
            loads(sync, 0, low_loaded)

        @block.gpsimd
        def _(pool):
            nc.gpsimd.memset(identity[:], 0.0).then_inc(zeroed, 1)
            pool.wait_ge(zeroed, 1)
            nc.gpsimd.affine_select(
                out=identity[:], in_=identity[:], compare_op=NOT_EQUAL, fill=1.0, base=0, pattern=[[-1, PARTS]],
                channel_multiplier=1).then_inc(identity_ready, 1)
            loads(pool, 1, high_loaded)

        @block.scalar
        def _(act):
            def cross(n, k):
                act.wait_ge(low_loaded[k], (n + 1) * 32)
                nc.scalar.copy(x_in[HALF:PARTS, k, 0, :, 0:KEPT], x_in[0:HALF, k, 0, :, KEPT:RUN])
                act.wait_ge(high_loaded[k], (n + 1) * 32)
                nc.scalar.copy(x_in[0:HALF, k, 1, :, 0:KEPT], x_in[HALF:PARTS, k, 1, :, KEPT:RUN]).then_inc(crossed, 1)

            def pack(group, chunk):
                act.wait_ge(unpaired, group * CHUNKS + chunk + 1)
                for i in range(max(1, chunk * PER_CHUNK), (chunk + 1) * PER_CHUNK):
                    at = first_column(i)
                    last = nc.scalar.copy(packed_rows[:, :, at:at + i],
                                          unpaired_banks[chunk % CHUNK_BANKS][:, i % PER_CHUNK, :, 0:i])
                last.then_inc(packed, 1)

            def store(group):
                act.wait_ge(packed, (group + 1) * CHUNKS)
                for side in range(SIDES):
                    act.dma_start(y[bass.ds(group * (SIDES * GROUP_PAIRS) + side * GROUP_PAIRS, GROUP_PAIRS), :],
                                  packed_rows[:, side, :]).then_inc(stored, 16)

            def quartet(group, q, last_group):
                n = group * QUARTETS + q
                if last_group is None:
                    for k in range(RING):
                        cross(n, k)
                else:
                    for k in range(RING - 1):
                        cross(n, k)
                    if not is_zero(last_group):
                        act.wait_ge(stored, last_group * 32)
                    for chunk in range(CHUNKS_PER_TILE):
                        pack(last_group, chunk)
                    cross(n, RING - 1)
                    for chunk in range(CHUNKS_PER_TILE, CHUNKS):
                        pack(last_group, chunk)
                    store(last_group)

            walk(act, quartet)
            act.wait_ge(stored, (GROUPS - 1) * 32)
            for chunk in range(CHUNKS):
                pack(GROUPS - 1, chunk)
            store(GROUPS - 1)
            act.wait_ge(stored, GROUPS * 32)

        @block.vector
        def _(dve):
            def turn(n, k):
                dve.wait_ge(crossed, n * RING + k + 1)
                if not is_zero(n):
                    dve.wait_ge(multiplied, n * RING + k - RING + 1)
                for step in range(KSTEPS):
                    last = nc.vector.transpose(
                        x_turned[:, k, :, step, :],
                        x_in[:, k, :, :, step * BLOCK:(step + 1) * BLOCK].rearrange("p s r c -> p (s r) c"))
                last.then_inc(turned, 1)

            def keep(n, k, tile):
                dve.wait_ge(multiplied, n * RING + k + 1)
                nc.vector.tensor_copy(products[:, :, bass.ds(tile * PAIRS, PAIRS)],
                                      product_banks[k][:].rearrange("p b i -> p i b")).then_inc(kept, 1)

            def quartet(group, q, last_group):
                n = group * QUARTETS + q
                first_quartet = is_zero(q)
                for k in range(RING):
                    turn(n, k)
                    if k < KEEP_LAG and not is_zero(n):
                        tile = (TILES if first_quartet else q * RING) + k - KEEP_LAG
                        keep(n - 1, k - KEEP_LAG + RING, tile)
                    elif k >= KEEP_LAG and not first_quartet:
                        keep(n, k - KEEP_LAG, q * RING + k - KEEP_LAG)
                if first_quartet:
                    if last_group is not None:
                        dve.wait_ge(unpaired, (last_group + 1) * CHUNKS)
                    for k in range(RING - KEEP_LAG):
                        keep(n, k, k)

            walk(dve, quartet)
            for k in range(RING - KEEP_LAG, RING):
                keep(GROUPS * QUARTETS - 1, k, TILES - RING + k)

        @block.tensor
        def _(pe):
            def multiply(n, k):
                pe.wait_ge(turned, n * RING + k + 1)
                if not is_zero(n):
                    pe.wait_ge(kept, n * RING + k - RING + 1)
                for side in range(SIDES):
                    for pair in range(PAIRS):
                        for step in range(KSTEPS):
                            rows = x_turned[:, k, side * PAIRS + pair, step, :]
                            last = nc.tensor.matmul(product_banks[k][side * HALF:(side + 1) * HALF, pair, :],
                                                    rows, rows, start=step == 0, stop=step == KSTEPS - 1)
                last.then_inc(multiplied, 1)

            def unpair(group, chunk):
                if not is_zero(group) or chunk >= CHUNK_BANKS:
                    pe.wait_ge(packed, group * CHUNKS + max(0, chunk - CHUNK_BANKS + 1))
                for i in range(max(1, chunk * PER_CHUNK), (chunk + 1) * PER_CHUNK):
                    last = nc.tensor.transpose(
                        unpaired_banks[chunk % CHUNK_BANKS][:, i % PER_CHUNK].rearrange("p s j -> p (s j)"),
                        products[:, i, :], identity[:])
                last.then_inc(unpaired, 1)

            def quartet(group, q, last_group):
                n = group * QUARTETS + q
                for k in range(RING):
                    multiply(n, k)
                    if last_group is not None and k < UNPAIR_TILES:
                        if k == 0:
                            pe.wait_ge(kept, (last_group + 1) * TILES)
                        for chunk in range(k * CHUNKS_PER_TILE, (k + 1) * CHUNKS_PER_TILE):
                            unpair(last_group, chunk)

            pe.wait_ge(identity_ready, 1)
            walk(pe, quartet)
            pe.wait_ge(kept, GROUPS * TILES)
            for chunk in range(CHUNKS):
                unpair(GROUPS - 1, chunk)


def kernel(r_inputs):
    import numpy as np
    from concourse import bacc
    from concourse.bass_utils import run_bass_kernel_spmd

    x = np.ascontiguousarray(r_inputs)
    batches, rows, _ = x.shape
    nc = bacc.Bacc("TRN2", target_bir_lowering=False, num_devices=1)
    x_dram = nc.dram_tensor("x_dram", x.shape, F32, kind="ExternalInput").ap()
    y_dram = nc.dram_tensor("y_dram", (batches, rows * (rows - 1) // 2), F32, kind="ExternalOutput").ap()
    gram_lower_triangle(nc, x_dram, y_dram)
    result = run_bass_kernel_spmd(nc, [{"x_dram": x}], core_ids=[0])
    return result.results[0]["y_dram"]
```

```python
from contextlib import ExitStack

import concourse.bass as bass
from concourse import mybir

F32 = mybir.dt.float32
NOT_EQUAL = mybir.AluOpType.not_equal

PARTS = 128
HALF = PARTS // 2
BLOCK = 32


def first_column(i):
    return i * (i - 1) // 2


def is_zero(value):
    return isinstance(value, int) and value == 0


def gram_lower_triangle(nc: bass.Bass, x: bass.AP, y: bass.AP):
    BATCHES, ROWS, DIM = x.shape
    PACKED = y.shape[1]
    SIDES = 2
    RUN = DIM // 2
    KEPT = RUN // 2
    KSTEPS = KEPT // BLOCK
    PAIRS = 8
    SLOTS = PAIRS * (ROWS // BLOCK)
    GROUP_PAIRS = PARTS
    RING = 4
    TILES = GROUP_PAIRS // PAIRS
    QUARTETS = TILES // RING
    GROUPS = BATCHES // (SIDES * GROUP_PAIRS)
    PER_CHUNK = 4
    CHUNKS = ROWS // PER_CHUNK
    CHUNK_BANKS = 4
    KEEP_LAG = 2
    UNPAIR_BEHIND = (1, 2)
    CHUNKS_PER_TILE = CHUNKS // len(UNPAIR_BEHIND)
    STORED_COLUMNS = PACKED // QUARTETS
    LAST_PIECES = (12, 8, 4, 0)

    with ExitStack() as stack:
        def sbuf(name, shape):
            return stack.enter_context(nc.sbuf_tensor(name, shape, F32))

        def psum(name, shape):
            return stack.enter_context(nc.psum_tensor(name, shape, F32))

        def semaphore(name):
            return stack.enter_context(nc.semaphore(name))

        x_in = sbuf("x_in", [PARTS, RING, SIDES, SLOTS, RUN])
        x_turned = sbuf("x_turned", [PARTS, RING, SIDES * PAIRS, KSTEPS, ROWS])
        products = sbuf("products", [PARTS, ROWS, GROUP_PAIRS])
        packed_rows = sbuf("packed_rows", [PARTS, SIDES, PACKED])
        identity = sbuf("identity", [PARTS, PARTS])
        product_banks = [psum(f"product_bank{k}", [PARTS, PAIRS, ROWS]) for k in range(RING)]
        unpaired_banks = [psum(f"unpaired_bank{k}", [PARTS, PER_CHUNK, SIDES, ROWS]) for k in range(CHUNK_BANKS)]

        low_loaded = [semaphore(f"low_loaded{k}") for k in range(RING)]
        high_loaded = [semaphore(f"high_loaded{k}") for k in range(RING)]
        crossed = semaphore("crossed")
        turned = semaphore("turned")
        multiplied = semaphore("multiplied")
        kept = semaphore("kept")
        unpaired = semaphore("unpaired")
        packed = semaphore("packed")
        stored = semaphore("stored")
        zeroed = semaphore("zeroed")
        identity_ready = semaphore("identity_ready")

        block = stack.enter_context(nc.Block())

        def walk(engine, quartet):
            quartet(0, 0, None)
            with engine.Fori(1, QUARTETS) as q:
                quartet(0, q, None)
            quartet(1, 0, 0)
            with engine.Fori(1, GROUPS - 1) as group:
                with engine.Fori(1, QUARTETS) as q:
                    quartet(group, q, group - 1)
                quartet(group + 1, 0, group)
            with engine.Fori(1, QUARTETS) as q:
                quartet(GROUPS - 1, q, GROUPS - 2)

        def load_tile(engine, side, first, k, loaded):
            for d_half in range(2):
                at = side * HALF + d_half * BLOCK
                source = x[bass.ds(first, PAIRS), :, d_half * RUN:(d_half + 1) * RUN].rearrange(
                    "b (h r) d -> r (b h) d", r=BLOCK)
                engine.dma_start(x_in[at:at + BLOCK, k, side], source).then_inc(loaded[k], 16)

        def loads(engine, side, loaded):
            def quartet(group, q, last_group):
                n = group * QUARTETS + q
                for k in range(RING):
                    if not is_zero(n):
                        engine.wait_ge(turned, (n * RING + k - RING) * SIDES + side + 1)
                    first = (group * SIDES + side) * GROUP_PAIRS + (q * RING + k) * PAIRS
                    load_tile(engine, side, first, k, loaded)
            walk(engine, quartet)

        @block.sync
        def _(sync):
            loads(sync, 0, low_loaded)

        @block.gpsimd
        def _(pool):
            nc.gpsimd.memset(identity[:], 0.0).then_inc(zeroed, 1)
            pool.wait_ge(zeroed, 1)
            nc.gpsimd.affine_select(
                out=identity[:], in_=identity[:], compare_op=NOT_EQUAL, fill=1.0, base=0, pattern=[[-1, PARTS]],
                channel_multiplier=1).then_inc(identity_ready, 1)
            loads(pool, 1, high_loaded)

        @block.scalar
        def _(act):
            def cross(n, k):
                for side, loaded in ((0, low_loaded), (1, high_loaded)):
                    home, other = slice(side * HALF, (side + 1) * HALF), slice((1 - side) * HALF, (2 - side) * HALF)
                    act.wait_ge(loaded[k], (n + 1) * 32)
                    nc.scalar.copy(x_in[other, k, side, :, 0:KEPT],
                                   x_in[home, k, side, :, KEPT:RUN]).then_inc(crossed, 1)

            def pack(group, chunk, done=None):
                act.wait_ge(unpaired, group * CHUNKS + (done or chunk + 1))
                for i in range(max(1, chunk * PER_CHUNK), (chunk + 1) * PER_CHUNK):
                    at = first_column(i)
                    last = nc.scalar.copy(packed_rows[:, :, at:at + i],
                                          unpaired_banks[chunk % CHUNK_BANKS][:, i % PER_CHUNK, :, 0:i])
                last.then_inc(packed, 1)

            def store(group, start, columns):
                rows = y[bass.ds(group * (SIDES * GROUP_PAIRS), SIDES * GROUP_PAIRS), bass.ds(start, columns)]
                act.dma_start(rows.rearrange("(s p) c -> p s c", p=GROUP_PAIRS),
                              packed_rows[:, :, bass.ds(start, columns)]).then_inc(stored, 16)

            def quartet(group, q, last_group):
                n = group * QUARTETS + q
                if is_zero(q) and last_group is not None:
                    for k in range(RING - 1):
                        cross(n, k)
                    if not is_zero(last_group):
                        act.wait_ge(stored, last_group * (QUARTETS * 16))
                    for chunk in range(CHUNKS_PER_TILE):
                        pack(last_group, chunk)
                    cross(n, RING - 1)
                    for chunk in range(CHUNKS_PER_TILE, CHUNKS):
                        pack(last_group, chunk)
                    act.wait_ge(packed, (last_group + 1) * CHUNKS)
                else:
                    for k in range(RING):
                        cross(n, k)
                if last_group is not None:
                    store(last_group, q * STORED_COLUMNS, STORED_COLUMNS)

            walk(act, quartet)
            act.wait_ge(stored, (GROUPS - 1) * (QUARTETS * 16))
            end = PACKED
            for done, chunk in enumerate(reversed(range(CHUNKS)), start=1):
                pack(GROUPS - 1, chunk, done)
                if chunk in LAST_PIECES:
                    start = first_column(max(1, chunk * PER_CHUNK))
                    act.wait_ge(packed, (GROUPS - 1) * CHUNKS + done)
                    store(GROUPS - 1, start, end - start)
                    end = start
            act.wait_ge(stored, ((GROUPS - 1) * QUARTETS + len(LAST_PIECES)) * 16)

        @block.vector
        def _(dve):
            def turn(n, k):
                if not is_zero(n):
                    dve.wait_ge(multiplied, n * RING + k - RING + 1)
                for side in range(SIDES):
                    dve.wait_ge(crossed, (n * RING + k) * SIDES + side + 1)
                    nc.vector.transpose(x_turned[:, k, side * PAIRS:(side + 1) * PAIRS].rearrange("p b s (h r) -> p b h s r", r=BLOCK),
                                        x_in[:, k, side, :, 0:KEPT].rearrange("p (b h) (s r) -> p b h s r", b=PAIRS, r=BLOCK)).then_inc(turned, 1)

            def keep(n, k, tile):
                dve.wait_ge(multiplied, n * RING + k + 1)
                nc.vector.tensor_copy(products[:, :, bass.ds(tile * PAIRS, PAIRS)],
                                      product_banks[k][:].rearrange("p b i -> p i b")).then_inc(kept, 1)

            def quartet(group, q, last_group):
                n = group * QUARTETS + q
                first_quartet = is_zero(q)
                for k in range(RING):
                    turn(n, k)
                    if k < KEEP_LAG and not is_zero(n):
                        tile = (TILES if first_quartet else q * RING) + k - KEEP_LAG
                        keep(n - 1, k - KEEP_LAG + RING, tile)
                    elif k >= KEEP_LAG and not first_quartet:
                        keep(n, k - KEEP_LAG, q * RING + k - KEEP_LAG)
                if first_quartet:
                    if last_group is not None:
                        dve.wait_ge(unpaired, (last_group + 1) * CHUNKS)
                    for k in range(RING - KEEP_LAG):
                        keep(n, k, k)

            walk(dve, quartet)
            for k in range(RING - KEEP_LAG, RING):
                keep(GROUPS * QUARTETS - 1, k, TILES - RING + k)

        @block.tensor
        def _(pe):
            def multiply(n, k):
                if not is_zero(n):
                    pe.wait_ge(kept, n * RING + k - RING + 1)
                for side in range(SIDES):
                    pe.wait_ge(turned, (n * RING + k) * SIDES + side + 1)
                    for pair in range(PAIRS):
                        for step in range(KSTEPS):
                            rows = x_turned[:, k, side * PAIRS + pair, step, :]
                            last = nc.tensor.matmul(product_banks[k][side * HALF:(side + 1) * HALF, pair, :],
                                                    rows, rows, start=step == 0, stop=step == KSTEPS - 1)
                last.then_inc(multiplied, 1)

            def unpair(group, chunk, done=None):
                before = done - 1 if done else chunk
                if not is_zero(group) or before >= CHUNK_BANKS:
                    pe.wait_ge(packed, group * CHUNKS + max(0, before - CHUNK_BANKS + 1))
                for i in range(max(1, chunk * PER_CHUNK), (chunk + 1) * PER_CHUNK):
                    last = nc.tensor.transpose(
                        unpaired_banks[chunk % CHUNK_BANKS][:, i % PER_CHUNK].rearrange("p s j -> p (s j)"),
                        products[:, i, :], identity[:])
                last.then_inc(unpaired, 1)

            def quartet(group, q, last_group):
                n = group * QUARTETS + q
                for k in range(RING):
                    multiply(n, k)
                    if is_zero(q) and last_group is not None and k in UNPAIR_BEHIND:
                        pe.wait_ge(kept, (last_group + 1) * TILES)
                        turn_at = UNPAIR_BEHIND.index(k) * CHUNKS_PER_TILE
                        for chunk in range(turn_at, turn_at + CHUNKS_PER_TILE):
                            unpair(last_group, chunk)

            pe.wait_ge(identity_ready, 1)
            walk(pe, quartet)
            pe.wait_ge(kept, GROUPS * TILES)
            for done, chunk in enumerate(reversed(range(CHUNKS)), start=1):
                unpair(GROUPS - 1, chunk, done)


def kernel(r_inputs):
    import numpy as np
    from concourse import bacc
    from concourse.bass_utils import run_bass_kernel_spmd

    x = np.ascontiguousarray(r_inputs)
    batches, rows, _ = x.shape
    nc = bacc.Bacc("TRN2", target_bir_lowering=False, num_devices=1)
    x_dram = nc.dram_tensor("x_dram", x.shape, F32, kind="ExternalInput").ap()
    y_dram = nc.dram_tensor("y_dram", (batches, rows * (rows - 1) // 2), F32, kind="ExternalOutput").ap()
    gram_lower_triangle(nc, x_dram, y_dram)
    result = run_bass_kernel_spmd(nc, [{"x_dram": x}], core_ids=[0])
    return result.results[0]["y_dram"]
```

```python
from contextlib import ExitStack

import concourse.bass as bass
from concourse import mybir

F32 = mybir.dt.float32
NOT_EQUAL = mybir.AluOpType.not_equal

PARTS = 128
HALF = PARTS // 2
BLOCK = 32


def first_column(i):
    return i * (i - 1) // 2


def is_zero(value):
    return isinstance(value, int) and value == 0


def gram_lower_triangle(nc: bass.Bass, x: bass.AP, y: bass.AP):
    BATCHES, ROWS, DIM = x.shape
    PACKED = y.shape[1]
    SIDES = 2
    RUN = DIM // 2
    KEPT = RUN // 2
    KSTEPS = KEPT // BLOCK
    PAIRS = 8
    SLOTS = PAIRS * (ROWS // BLOCK)
    GROUP_PAIRS = PARTS
    RING = 4
    TILES = GROUP_PAIRS // PAIRS
    QUARTETS = TILES // RING
    GROUPS = BATCHES // (SIDES * GROUP_PAIRS)
    PER_CHUNK = 4
    CHUNKS = ROWS // PER_CHUNK
    CHUNK_BANKS = 4
    KEEP_LAG = 3
    UNPAIRED_BEHIND = (range(8), range(8, 16), (), ())
    PACKED_BEHIND = ((), range(4), range(4, 8), range(8, 16))
    PACKERS = 2
    STORES = QUARTETS - 1
    STORED_COLUMNS = PACKED // STORES
    STORE_BEHIND = 1
    LAST_PIECES = (3, 7, 11, 15)

    with ExitStack() as stack:
        def sbuf(name, shape):
            return stack.enter_context(nc.sbuf_tensor(name, shape, F32))

        def psum(name, shape):
            return stack.enter_context(nc.psum_tensor(name, shape, F32))

        def semaphore(name):
            return stack.enter_context(nc.semaphore(name))

        x_in = sbuf("x_in", [PARTS, RING, SIDES, SLOTS, RUN])
        x_turned = sbuf("x_turned", [PARTS, RING, SIDES * PAIRS, KSTEPS, ROWS])
        products = sbuf("products", [PARTS, ROWS, GROUP_PAIRS])
        packed_rows = sbuf("packed_rows", [PARTS, SIDES, PACKED])
        identity = sbuf("identity", [PARTS, PARTS])
        product_banks = [psum(f"product_bank{k}", [PARTS, PAIRS, ROWS]) for k in range(RING)]
        unpaired_banks = [psum(f"unpaired_bank{k}", [PARTS, PER_CHUNK, SIDES, ROWS]) for k in range(CHUNK_BANKS)]

        low_loaded = [semaphore(f"low_loaded{k}") for k in range(RING)]
        high_loaded = [semaphore(f"high_loaded{k}") for k in range(RING)]
        crossed = semaphore("crossed")
        turned = semaphore("turned")
        multiplied = semaphore("multiplied")
        kept = semaphore("kept")
        unpaired = semaphore("unpaired")
        packed = [semaphore("packed_by_scalar"), semaphore("packed_by_vector")]
        stored = semaphore("stored")
        zeroed = semaphore("zeroed")
        identity_ready = semaphore("identity_ready")

        block = stack.enter_context(nc.Block())

        def walk(engine, quartet):
            quartet(0, 0, None)
            with engine.Fori(1, QUARTETS) as q:
                quartet(0, q, None)
            quartet(1, 0, 0)
            with engine.Fori(1, GROUPS - 1) as group:
                with engine.Fori(1, QUARTETS) as q:
                    quartet(group, q, group - 1)
                quartet(group + 1, 0, group)
            with engine.Fori(1, QUARTETS) as q:
                quartet(GROUPS - 1, q, GROUPS - 2)

        def load_tile(engine, side, first, k, loaded):
            for d_half in range(2):
                at = side * HALF + d_half * BLOCK
                source = x[bass.ds(first, PAIRS), :, d_half * RUN:(d_half + 1) * RUN].rearrange(
                    "b (h r) d -> r (b h) d", r=BLOCK)
                engine.dma_start(x_in[at:at + BLOCK, k, side], source).then_inc(loaded[k], 16)

        def loads(engine, side, loaded):
            def quartet(group, q, last_group):
                n = group * QUARTETS + q
                for k in range(RING):
                    if not is_zero(n):
                        engine.wait_ge(turned, (n * RING + k - RING) * SIDES + side + 1)
                    first = (group * SIDES + side) * GROUP_PAIRS + (q * RING + k) * PAIRS
                    load_tile(engine, side, first, k, loaded)
            walk(engine, quartet)

        def rows_of_chunk(step):
            chunk = CHUNKS - 1 - step
            return range(max(1, chunk * PER_CHUNK), (chunk + 1) * PER_CHUNK)

        def pack(engine, copy, group, steps):
            mine = 0 if engine is nc.scalar else 1
            for step in steps:
                if step % PACKERS == mine:
                    engine.wait_ge(unpaired, group * CHUNKS + step + 1)
                    for i in rows_of_chunk(step):
                        start = first_column(i)
                        last = copy(packed_rows[:, :, start:start + i],
                                    unpaired_banks[step % CHUNK_BANKS][:, i % PER_CHUNK, :, 0:i])
                    last.then_inc(packed[mine], 1)

        @block.sync
        def _(sync):
            loads(sync, 0, low_loaded)

        @block.gpsimd
        def _(pool):
            nc.gpsimd.memset(identity[:], 0.0).then_inc(zeroed, 1)
            pool.wait_ge(zeroed, 1)
            nc.gpsimd.affine_select(
                out=identity[:], in_=identity[:], compare_op=NOT_EQUAL, fill=1.0, base=0, pattern=[[-1, PARTS]],
                channel_multiplier=1).then_inc(identity_ready, 1)
            loads(pool, 1, high_loaded)

        @block.scalar
        def _(act):
            def cross(n, k):
                for side, loaded in ((0, low_loaded), (1, high_loaded)):
                    home, other = slice(side * HALF, (side + 1) * HALF), slice((1 - side) * HALF, (2 - side) * HALF)
                    act.wait_ge(loaded[k], (n + 1) * 32)
                    nc.scalar.copy(x_in[other, k, side, :, 0:KEPT],
                                   x_in[home, k, side, :, KEPT:RUN]).then_inc(crossed, 1)

            def keep(n, k, tile):
                act.wait_ge(multiplied, n * RING + k + 1)
                nc.scalar.copy(products[:, :, bass.ds(tile * PAIRS, PAIRS)],
                               product_banks[k][:].rearrange("p b i -> p i b")).then_inc(kept, 1)

            def store(group, start, columns):
                rows = y[bass.ds(group * (SIDES * GROUP_PAIRS), SIDES * GROUP_PAIRS), bass.ds(start, columns)]
                act.dma_start(rows.rearrange("(s p) c -> p s c", p=GROUP_PAIRS),
                              packed_rows[:, :, bass.ds(start, columns)]).then_inc(stored, 16)

            def quartet(group, q, last_group):
                n = group * QUARTETS + q
                first_quartet = is_zero(q)
                unpairing = first_quartet and last_group is not None
                if unpairing and not is_zero(last_group):
                    act.wait_ge(stored, last_group * (STORES * 16))
                for k in range(RING):
                    cross(n, k)
                    if unpairing:
                        pack(nc.scalar, nc.scalar.copy, last_group, PACKED_BEHIND[k])
                    if k == STORE_BEHIND and not is_zero(q) and last_group is not None:
                        for by in packed:
                            act.wait_ge(by, (last_group + 1) * (CHUNKS // PACKERS))
                        store(last_group, (q - 1) * STORED_COLUMNS, STORED_COLUMNS)
                    if not first_quartet:
                        if k < KEEP_LAG:
                            keep(n - 1, k - KEEP_LAG + RING, q * RING + k - KEEP_LAG)
                        else:
                            keep(n, k - KEEP_LAG, q * RING + k - KEEP_LAG)
                    elif unpairing and k == 0:
                        for lag in range(KEEP_LAG, 0, -1):
                            keep(n - 1, RING - lag, TILES - lag)
                if first_quartet:
                    if unpairing:
                        act.wait_ge(unpaired, (last_group + 1) * CHUNKS)
                    for k in range(RING - KEEP_LAG):
                        keep(n, k, k)

            walk(act, quartet)
            for k in range(RING - KEEP_LAG, RING):
                keep(GROUPS * QUARTETS - 1, k, TILES - RING + k)
            act.wait_ge(stored, (GROUPS - 1) * (STORES * 16))
            end = PACKED
            for step in range(CHUNKS):
                pack(nc.scalar, nc.scalar.copy, GROUPS - 1, [step])
                if step in LAST_PIECES:
                    start = first_column(rows_of_chunk(step)[0])
                    for by in packed:
                        act.wait_ge(by, (GROUPS - 1) * (CHUNKS // PACKERS) + (step + 1) // PACKERS)
                    store(GROUPS - 1, start, end - start)
                    end = start
            act.wait_ge(stored, ((GROUPS - 1) * STORES + len(LAST_PIECES)) * 16)

        @block.vector
        def _(dve):
            def turn(n, k):
                if not is_zero(n):
                    dve.wait_ge(multiplied, n * RING + k - RING + 1)
                for side in range(SIDES):
                    dve.wait_ge(crossed, (n * RING + k) * SIDES + side + 1)
                    turned_blocks = x_turned[:, k, side * PAIRS:(side + 1) * PAIRS].rearrange(
                        "p b s (h r) -> p b h s r", r=BLOCK)
                    blocks = x_in[:, k, side, :, 0:KEPT].rearrange("p (b h) (s r) -> p b h s r", b=PAIRS, r=BLOCK)
                    nc.vector.transpose(turned_blocks, blocks).then_inc(turned, 1)

            def quartet(group, q, last_group):
                n = group * QUARTETS + q
                unpairing = is_zero(q) and last_group is not None
                if unpairing and not is_zero(last_group):
                    dve.wait_ge(stored, last_group * (STORES * 16))
                for k in range(RING):
                    turn(n, k)
                    if unpairing:
                        pack(nc.vector, nc.vector.tensor_copy, last_group, PACKED_BEHIND[k])

            walk(dve, quartet)
            dve.wait_ge(stored, (GROUPS - 1) * (STORES * 16))
            pack(nc.vector, nc.vector.tensor_copy, GROUPS - 1, range(CHUNKS))

        @block.tensor
        def _(pe):
            def multiply(n, k):
                if not is_zero(n):
                    pe.wait_ge(kept, n * RING + k - RING + 1)
                for side in range(SIDES):
                    pe.wait_ge(turned, (n * RING + k) * SIDES + side + 1)
                    for pair in range(PAIRS):
                        for step in range(KSTEPS):
                            rows = x_turned[:, k, side * PAIRS + pair, step, :]
                            last = nc.tensor.matmul(product_banks[k][side * HALF:(side + 1) * HALF, pair, :],
                                                    rows, rows, start=step == 0, stop=step == KSTEPS - 1)
                last.then_inc(multiplied, 1)

            def unpair(group, step):
                if not is_zero(group) or step >= CHUNK_BANKS:
                    pe.wait_ge(packed[step % PACKERS],
                               group * (CHUNKS // PACKERS) + max(0, (step - CHUNK_BANKS) // PACKERS + 1))
                for i in rows_of_chunk(step):
                    last = nc.tensor.transpose(
                        unpaired_banks[step % CHUNK_BANKS][:, i % PER_CHUNK].rearrange("p s j -> p (s j)"),
                        products[:, i, :], identity[:])
                last.then_inc(unpaired, 1)

            def quartet(group, q, last_group):
                n = group * QUARTETS + q
                for k in range(RING):
                    multiply(n, k)
                    if is_zero(q) and last_group is not None:
                        pe.wait_ge(kept, (last_group + 1) * TILES)
                        for step in UNPAIRED_BEHIND[k]:
                            unpair(last_group, step)

            pe.wait_ge(identity_ready, 1)
            walk(pe, quartet)
            pe.wait_ge(kept, GROUPS * TILES)
            for step in range(CHUNKS):
                unpair(GROUPS - 1, step)


def kernel(r_inputs):
    import numpy as np
    from concourse import bacc
    from concourse.bass_utils import run_bass_kernel_spmd

    x = np.ascontiguousarray(r_inputs)
    batches, rows, _ = x.shape
    nc = bacc.Bacc("TRN2", target_bir_lowering=False, num_devices=1)
    x_dram = nc.dram_tensor("x_dram", x.shape, F32, kind="ExternalInput").ap()
    y_dram = nc.dram_tensor("y_dram", (batches, rows * (rows - 1) // 2), F32, kind="ExternalOutput").ap()
    gram_lower_triangle(nc, x_dram, y_dram)
    result = run_bass_kernel_spmd(nc, [{"x_dram": x}], core_ids=[0])
    return result.results[0]["y_dram"]
```
